# Optimizing a Trainium2 kernel written in Bass

```python
import numpy as np
import jax
import jax.numpy as jnp

def _softmax(x, axis=-1):
    return jax.nn.softmax(x, axis=axis)

def _gelu(x):
    return jax.nn.gelu(x, approximate=True)

def _silu(x):
    return jax.nn.silu(x)

def _sigmoid(x):
    return jax.nn.sigmoid(x)

def _layernorm(x, axis=-1, eps=1e-05):
    m = jnp.mean(x, axis=axis, keepdims=True)
    v = jnp.var(x, axis=axis, keepdims=True)
    return (x - m) / jnp.sqrt(v + eps)

def _scatter_add(tgt, idx, src, axis=0):
    return tgt.at[idx].add(src)

def _segment_sum(src, seg, n):
    return jax.ops.segment_sum(src, seg, n)
kernel_name = 'mk_dlrm_tower_d1_rec_r8_579097'

def setup_inputs(seed: int=0):
    np.random.seed(seed)
    _w = jnp.asarray

    def _rec_inputs():
        import jax
        import jax.numpy as jnp
        _tk = jax.random.key(seed)
        ids = jnp.stack([jax.random.randint(jax.random.fold_in(_tk, 200 + f), (2048,), 0, v, jnp.int32) for f, v in enumerate([1250, 12500, 1250, 1250, 125000, 1250, 1000, 1000, 1250, 1000, 12500, 12500, 1000, 1250, 1000, 1000, 1250, 1000, 1000, 1250, 1000, 1000, 12500, 1250, 12500, 12500])], axis=1)
        tbl_0 = 0.05 * jax.random.normal(jax.random.fold_in(_tk, 500 + 0), (1250, 128), jnp.float32)
        tbl_1 = 0.05 * jax.random.normal(jax.random.fold_in(_tk, 500 + 1), (12500, 128), jnp.float32)
        tbl_2 = 0.05 * jax.random.normal(jax.random.fold_in(_tk, 500 + 2), (1250, 128), jnp.float32)
        tbl_3 = 0.05 * jax.random.normal(jax.random.fold_in(_tk, 500 + 3), (1250, 128), jnp.float32)
        tbl_4 = 0.05 * jax.random.normal(jax.random.fold_in(_tk, 500 + 4), (125000, 128), jnp.float32)
        tbl_5 = 0.05 * jax.random.normal(jax.random.fold_in(_tk, 500 + 5), (1250, 128), jnp.float32)
        tbl_6 = 0.05 * jax.random.normal(jax.random.fold_in(_tk, 500 + 6), (1000, 128), jnp.float32)
        tbl_7 = 0.05 * jax.random.normal(jax.random.fold_in(_tk, 500 + 7), (1000, 128), jnp.float32)
        tbl_8 = 0.05 * jax.random.normal(jax.random.fold_in(_tk, 500 + 8), (1250, 128), jnp.float32)
        tbl_9 = 0.05 * jax.random.normal(jax.random.fold_in(_tk, 500 + 9), (1000, 128), jnp.float32)
        tbl_10 = 0.05 * jax.random.normal(jax.random.fold_in(_tk, 500 + 10), (12500, 128), jnp.float32)
        tbl_11 = 0.05 * jax.random.normal(jax.random.fold_in(_tk, 500 + 11), (12500, 128), jnp.float32)
        tbl_12 = 0.05 * jax.random.normal(jax.random.fold_in(_tk, 500 + 12), (1000, 128), jnp.float32)
        tbl_13 = 0.05 * jax.random.normal(jax.random.fold_in(_tk, 500 + 13), (1250, 128), jnp.float32)
        tbl_14 = 0.05 * jax.random.normal(jax.random.fold_in(_tk, 500 + 14), (1000, 128), jnp.float32)
        tbl_15 = 0.05 * jax.random.normal(jax.random.fold_in(_tk, 500 + 15), (1000, 128), jnp.float32)
        tbl_16 = 0.05 * jax.random.normal(jax.random.fold_in(_tk, 500 + 16), (1250, 128), jnp.float32)
        tbl_17 = 0.05 * jax.random.normal(jax.random.fold_in(_tk, 500 + 17), (1000, 128), jnp.float32)
        tbl_18 = 0.05 * jax.random.normal(jax.random.fold_in(_tk, 500 + 18), (1000, 128), jnp.float32)
        tbl_19 = 0.05 * jax.random.normal(jax.random.fold_in(_tk, 500 + 19), (1250, 128), jnp.float32)
        tbl_20 = 0.05 * jax.random.normal(jax.random.fold_in(_tk, 500 + 20), (1000, 128), jnp.float32)
        tbl_21 = 0.05 * jax.random.normal(jax.random.fold_in(_tk, 500 + 21), (1000, 128), jnp.float32)
        tbl_22 = 0.05 * jax.random.normal(jax.random.fold_in(_tk, 500 + 22), (12500, 128), jnp.float32)
        tbl_23 = 0.05 * jax.random.normal(jax.random.fold_in(_tk, 500 + 23), (1250, 128), jnp.float32)
        tbl_24 = 0.05 * jax.random.normal(jax.random.fold_in(_tk, 500 + 24), (12500, 128), jnp.float32)
        tbl_25 = 0.05 * jax.random.normal(jax.random.fold_in(_tk, 500 + 25), (12500, 128), jnp.float32)
        _rk = jax.random.fold_in(_tk, 7)
        r_dense_features = 7.22013e-05 + 1.00017 * jax.random.normal(jax.random.fold_in(_rk, 101), (2048, 128), jnp.float32)
        W_top1 = 0.0456912 * jax.random.normal(jax.random.fold_in(_tk, 801), (479, 512), jnp.float32)
        W_top2 = 0.0441942 * jax.random.normal(jax.random.fold_in(_tk, 802), (512, 256), jnp.float32)
        W_top3 = 0.0625 * jax.random.normal(jax.random.fold_in(_tk, 803), (256, 1), jnp.float32)
        b_top1 = jnp.zeros((512,), jnp.float32)
        b_top2 = jnp.zeros((256,), jnp.float32)
        return (r_dense_features, ids, tbl_0, tbl_1, tbl_2, tbl_3, tbl_4, tbl_5, tbl_6, tbl_7, tbl_8, tbl_9, tbl_10, tbl_11, tbl_12, tbl_13, tbl_14, tbl_15, tbl_16, tbl_17, tbl_18, tbl_19, tbl_20, tbl_21, tbl_22, tbl_23, tbl_24, tbl_25, W_top1, b_top1, W_top2, b_top2, W_top3)
    r_dense_features, ids, tbl_0, tbl_1, tbl_2, tbl_3, tbl_4, tbl_5, tbl_6, tbl_7, tbl_8, tbl_9, tbl_10, tbl_11, tbl_12, tbl_13, tbl_14, tbl_15, tbl_16, tbl_17, tbl_18, tbl_19, tbl_20, tbl_21, tbl_22, tbl_23, tbl_24, tbl_25, W_top1, b_top1, W_top2, b_top2, W_top3 = _rec_inputs()

    def _L0_rec_setup():
        import jax, jax.numpy as jnp
        import numpy as np
        FEATURE_NUM = 27
        key = jax.random.key(seed)
        k1, k2 = jax.random.split(key)
        B, N, D = (8192, FEATURE_NUM - 1, 128)
        dense_features = jax.random.normal(k1, (B, D), dtype=jnp.float32)
        sparse_features = jax.random.normal(k2, (B, N, D), dtype=jnp.float32)
        return {'dense_features': dense_features, 'sparse_features': sparse_features}
    _L0_rec_all = _L0_rec_setup()
    _L0_rec_in = {k: v for k, v in _L0_rec_all.items() if k in ()}
    del _L0_rec_all
    return {'r_dense_features': r_dense_features, 'ids': ids, 'tbl_0': tbl_0, 'tbl_1': tbl_1, 'tbl_2': tbl_2, 'tbl_3': tbl_3, 'tbl_4': tbl_4, 'tbl_5': tbl_5, 'tbl_6': tbl_6, 'tbl_7': tbl_7, 'tbl_8': tbl_8, 'tbl_9': tbl_9, 'tbl_10': tbl_10, 'tbl_11': tbl_11, 'tbl_12': tbl_12, 'tbl_13': tbl_13, 'tbl_14': tbl_14, 'tbl_15': tbl_15, 'tbl_16': tbl_16, 'tbl_17': tbl_17, 'tbl_18': tbl_18, 'tbl_19': tbl_19, 'tbl_20': tbl_20, 'tbl_21': tbl_21, 'tbl_22': tbl_22, 'tbl_23': tbl_23, 'tbl_24': tbl_24, 'tbl_25': tbl_25, 'W_top1': W_top1, 'b_top1': b_top1, 'W_top2': W_top2, 'b_top2': b_top2, 'W_top3': W_top3}

def reference(r_dense_features, ids, tbl_0, tbl_1, tbl_2, tbl_3, tbl_4, tbl_5, tbl_6, tbl_7, tbl_8, tbl_9, tbl_10, tbl_11, tbl_12, tbl_13, tbl_14, tbl_15, tbl_16, tbl_17, tbl_18, tbl_19, tbl_20, tbl_21, tbl_22, tbl_23, tbl_24, tbl_25, W_top1, b_top1, W_top2, b_top2, W_top3):
    import jax
    import jax.numpy as jnp

    def _L0_rec_ref(dense_features, sparse_features):
        import jax, jax.numpy as jnp
        import numpy as np
        FEATURE_NUM = 27
        combined = jnp.concatenate([dense_features[:, None, :], sparse_features], axis=1)
        interactions = jnp.einsum('bfd,bgd->bfg', combined, combined)
        iu, ju = jnp.triu_indices(FEATURE_NUM, k=1)
        return interactions[:, iu, ju]
    e = jnp.stack([tbl_0[ids[:, 0]], tbl_1[ids[:, 1]], tbl_2[ids[:, 2]], tbl_3[ids[:, 3]], tbl_4[ids[:, 4]], tbl_5[ids[:, 5]], tbl_6[ids[:, 6]], tbl_7[ids[:, 7]], tbl_8[ids[:, 8]], tbl_9[ids[:, 9]], tbl_10[ids[:, 10]], tbl_11[ids[:, 11]], tbl_12[ids[:, 12]], tbl_13[ids[:, 13]], tbl_14[ids[:, 14]], tbl_15[ids[:, 15]], tbl_16[ids[:, 16]], tbl_17[ids[:, 17]], tbl_18[ids[:, 18]], tbl_19[ids[:, 19]], tbl_20[ids[:, 20]], tbl_21[ids[:, 21]], tbl_22[ids[:, 22]], tbl_23[ids[:, 23]], tbl_24[ids[:, 24]], tbl_25[ids[:, 25]]], axis=1)
    z = _L0_rec_ref(r_dense_features, e)
    z = z.reshape(z.shape[0], -1)
    h = jnp.concatenate([z, r_dense_features], axis=1)
    h = jnp.maximum(h @ W_top1 + b_top1, 0.0)
    h = jnp.maximum(h @ W_top2 + b_top2, 0.0)
    y = h @ W_top3
    return y

_drawn_inputs = setup_inputs


def setup_inputs(seed=0):
    import zlib

    import numpy as np

    out = dict(_drawn_inputs(seed))
    spreads = {'b_top1': (0.0, 0.1), 'b_top2': (0.0, 0.1)}
    factors = {}
    for name, (base, spread) in spreads.items():
        noise = np.random.default_rng([zlib.crc32(name.encode()), seed]).standard_normal(out[name].shape)
        drawn = base * np.exp(spread * noise) if base else spread * noise
        out[name] = jnp.asarray(drawn.astype(out[name].dtype))
    for name, factor in factors.items():
        out[name] = (out[name] * factor).astype(out[name].dtype)
    return out
```

```python
import concourse.bass as bass
from concourse import mybir
from contextlib import ExitStack

BATCH = 2048
DIM = 128
N_TABLES = 26
FEATURES = N_TABLES + 1
HIDDEN1 = 512
HIDDEN2 = 256

TILE = 128
N_TILES = BATCH // TILE
SLOTS = 2
GROUPS = N_TILES // SLOTS
GCOLS = SLOTS * TILE

PER_BANK = 512 // TILE
T_BATCHES = -(-FEATURES // PER_BANK)

ROWS = 32
PACK = 128 // ROWS
GMM = TILE // PACK
CHUNK = 8
CHUNKS = GMM // CHUNK
PAIR_G = FEATURES - 1

PAIRS = FEATURES * (FEATURES - 1) // 2
PAIR_KT = -(-PAIRS // 128)
KT1 = PAIR_KT + 1
M1 = HIDDEN1 // 128
M2 = HIDDEN2 // 128


def pair_moves():
    moves, row = [], 0
    for f in range(FEATURES - 1):
        g = f
        while g < PAIR_G:
            n = min(PAIR_G - g, 128 - row % 128)
            moves.append((f, g, n, row // 128, row % 128))
            g += n
            row += n
    return moves


MOVES = pair_moves()


def build(nc, dense, ids, tables, w1, b1, w2, b2, w3, out):
    fp32 = mybir.dt.float32
    i32 = mybir.dt.int32
    ALU = mybir.AluOpType
    ACT = mybir.ActivationFunctionType

    dense_v = dense.rearrange("(p t) d -> p t d", t=N_TILES)
    ids_v = ids.rearrange("(p t) f -> p (t f)", t=N_TILES)
    out_v = out.rearrange("(p t) o -> p (t o)", t=N_TILES)

    ctx = ExitStack()
    with ctx:
        def sb(name, shape, dt=fp32):
            return ctx.enter_context(nc.sbuf_tensor(name, shape, dt))

        def pb(name, shape):
            return ctx.enter_context(nc.psum_tensor(name, shape, fp32))

        def sem(name):
            return ctx.enter_context(nc.semaphore(name))

        ids_all = sb("ids_all", [128, N_TILES * N_TABLES], i32)
        ids_tile = sb("ids_tile", [128, SLOTS, N_TABLES], i32)
        emb = sb("emb", [128, SLOTS, N_TABLES, DIM])
        dns = sb("dns", [128, SLOTS, DIM])
        featT = [sb(f"featT{b}", [128, TILE, ROWS]) for b in range(SLOTS)]
        denseT = sb("denseT", [128, BATCH])
        gram = sb("gram", [PAIR_G, PAIR_G, GCOLS])
        pairsT = sb("pairsT", [128, PAIR_KT, GCOLS])
        h1 = sb("h1", [128, M1, GCOLS])
        h2 = sb("h2", [128, M2, GCOLS])
        y = sb("y", [128, N_TILES])
        w1_sb = sb("w1_sb", [128, KT1, HIDDEN1])
        w2_sb = sb("w2_sb", [128, M1, HIDDEN2])
        w3_sb = sb("w3_sb", [128, M2])
        b1_sb = sb("b1_sb", [128, M1])
        b2_sb = sb("b2_sb", [128, M2])
        ident = sb("ident", [128, 128])

        ps_t = [pb(f"ps_t{i}", [128, PER_BANK, TILE]) for i in range(2)]
        ps_g = [pb(f"ps_g{i}", [128, CHUNK, 128]) for i in range(2)]
        ps_m = [pb(f"ps_m{i}", [128, 512]) for i in range(2)]

        ids_loaded = sem("ids_loaded")
        ids_copied = sem("ids_copied")
        pool_passed = sem("pool_passed")
        sp_passed = sem("sp_passed")
        gathered = [sem(f"gathered{b}") for b in range(SLOTS)]
        dense_loaded = [sem(f"dense_loaded{b}") for b in range(SLOTS)]
        weights_loaded = sem("weights_loaded")
        biases_loaded = sem("biases_loaded")
        ident_ready = sem("ident_ready")
        pads_zeroed = sem("pads_zeroed")
        transposed = sem("transposed")
        feat_copied = sem("feat_copied")
        gram_made = sem("gram_made")
        gram_copied = sem("gram_copied")
        pairs_packed = sem("pairs_packed")
        h1_made = sem("h1_made")
        h1_copied = sem("h1_copied")
        h2_made = sem("h2_made")
        h2_copied = sem("h2_copied")
        y_made = sem("y_made")
        y_copied = sem("y_copied")
        out_stored = sem("out_stored")

        block = ctx.enter_context(nc.Block())

        @block.sync
        def _(sp):
            def load_dense(t, b):
                sp.dma_start(dns[:, b, :], dense_v[:, bass.ds(t, 1), :]).then_inc(dense_loaded[b], 16)

            def pack_pairs(q, first=False):
                sp.wait_ge(gram_copied, SLOTS * CHUNKS * (q + 1))
                sp.sem_inc(sp_passed)
                if not first:
                    sp.wait_ge(h1_made, M1 * q)
                    sp.sem_inc(sp_passed)
                for f, g, n, kt, row in MOVES:
                    sp.dma_start(pairsT[row:row + n, kt, :], gram[f:f + 1, g:g + n, :]).then_inc(pairs_packed, 16)

            def next_dense(q):
                for b in range(SLOTS):
                    sp.wait_ge(transposed, T_BATCHES * (SLOTS * q + b + 1))
                    sp.sem_inc(sp_passed)
                    load_dense(SLOTS * (q + 1) + b, b)

            sp.dma_start(ids_all[:, :], ids_v).then_inc(ids_loaded, 16)
            for b in range(SLOTS):
                load_dense(b, b)
            for kt in range(PAIR_KT):
                n = min(128, PAIRS - kt * 128)
                sp.dma_start(w1_sb[0:n, kt, :], w1[kt * 128:kt * 128 + n, :]).then_inc(weights_loaded, 16)
            sp.dma_start(w1_sb[:, PAIR_KT, :], w1[PAIRS:PAIRS + DIM, :]).then_inc(weights_loaded, 16)
            sp.dma_start(w2_sb[:, :, :], w2.rearrange("(k p) n -> p k n", p=128)).then_inc(weights_loaded, 16)

            next_dense(0)
            pack_pairs(0, first=True)
            with sp.Fori(1, GROUPS - 1) as q:
                next_dense(q)
                pack_pairs(q)
            pack_pairs(GROUPS - 1)
            sp.wait_ge(y_copied, GROUPS)
            sp.dma_start(out_v, y[:, :]).then_inc(out_stored, 16)
            sp.wait_ge(out_stored, 16)

        @block.gpsimd
        def _(pool):
            pool.memset(ident[:, :], 0.0).then_inc(ident_ready, 1)
            pool.wait_ge(ident_ready, 1)
            pool.affine_select(out=ident[:, :], in_=ident[:, :], compare_op=ALU.not_equal, fill=1.0,
                               base=0, pattern=[[-1, 128]], channel_multiplier=1).then_inc(ident_ready, 1)

            def gather(q, b, first=False):
                t = SLOTS * q + b
                if not first:
                    pool.wait_ge(transposed, T_BATCHES * (t - SLOTS + 1))
                    pool.sem_inc(pool_passed)
                pool.tensor_copy(ids_tile[:, b, :], ids_all[:, bass.ds(t * N_TABLES, N_TABLES)]).then_inc(ids_copied, 1)
                pool.wait_ge(ids_copied, t + 1)
                pool.sem_inc(pool_passed)
                for f in range(N_TABLES):
                    pool.indirect_dma_start(
                        out=emb[:, b, f, :], out_offset=None, in_=tables[f][:, :],
                        in_offset=bass.IndirectOffsetOnAxis(ap=ids_tile[:, b, f:f + 1], axis=0),
                    ).then_inc(gathered[b], 16)

            pool.wait_ge(ids_loaded, 16)
            for b in range(SLOTS):
                gather(0, b, first=True)
            with pool.Fori(1, GROUPS) as q:
                for b in range(SLOTS):
                    gather(q, b)

        @block.tensor
        def _(pe):
            def transposes(q, b, first=False):
                pe.wait_ge(gathered[b], 16 * N_TABLES * (q + 1))
                pe.wait_ge(dense_loaded[b], 16 * (q + 1))
                for i in range(T_BATCHES):
                    n = b * T_BATCHES + i
                    if not (first and n < 2):
                        pe.wait_ge(feat_copied, SLOTS * T_BATCHES * q + n - 1)
                    for k in range(min(PER_BANK, FEATURES - i * PER_BANK)):
                        f = i * PER_BANK + k
                        src = dns[:, b, :] if f == 0 else emb[:, b, f - 1, :]
                        last = nc.tensor.transpose(ps_t[n % 2][:, k, :], src, ident[:, :])
                    last.then_inc(transposed, 1)

            def gram_products(q, b, first=False):
                pe.wait_ge(feat_copied, T_BATCHES * (SLOTS * q + b + 1))
                for c in range(CHUNKS):
                    n = b * CHUNKS + c
                    if not (first and n < 2):
                        pe.wait_ge(gram_copied, SLOTS * CHUNKS * q + n - 1)
                    for k in range(CHUNK):
                        s = (c * CHUNK + k) * PACK
                        last = nc.tensor.matmul(ps_g[n % 2][:, k, 0:PACK * PAIR_G], featT[b][:, s:s + PACK, :],
                                                featT[b][:, s:s + PACK, 1:FEATURES], start=True, stop=True)
                    last.then_inc(gram_made, 1)

            def layer1(q, first=False):
                pe.wait_ge(pairs_packed, 16 * len(MOVES) * (q + 1))
                for m in range(M1):
                    if m >= 2:
                        pe.wait_ge(h1_copied, M1 * q + m - 1)
                    elif not first and m == 0:
                        pe.wait_ge(y_copied, q)
                    elif not first and m == 1:
                        pe.wait_ge(h2_copied, M2 * q)
                    for kt in range(KT1):
                        n = min(128, PAIRS - kt * 128) if kt < PAIR_KT else 128
                        rhs = pairsT[0:n, kt, :] if kt < PAIR_KT else denseT[:, bass.ds(q * GCOLS, GCOLS)]
                        last = nc.tensor.matmul(ps_m[m % 2][:, 0:GCOLS], w1_sb[0:n, kt, m * 128:(m + 1) * 128], rhs,
                                                start=(kt == 0), stop=(kt == KT1 - 1))
                    last.then_inc(h1_made, 1)

            def layers23(q):
                for m in range(M2):
                    pe.wait_ge(h1_copied, M1 * (q + 1))
                    for kt in range(M1):
                        last = nc.tensor.matmul(ps_m[m % 2][:, 0:GCOLS], w2_sb[:, kt, m * 128:(m + 1) * 128],
                                                h1[:, kt, :], start=(kt == 0), stop=(kt == M1 - 1))
                    last.then_inc(h2_made, 1)
                pe.wait_ge(h2_copied, M2 * (q + 1))
                for b in range(SLOTS):
                    for kt in range(M2):
                        last = nc.tensor.matmul(ps_m[0][:, b:b + 1], h2[:, kt, b * TILE:(b + 1) * TILE],
                                                w3_sb[:, kt:kt + 1], start=(kt == 0), stop=(kt == M2 - 1))
                last.then_inc(y_made, 1)

            pe.wait_ge(ident_ready, 2)
            pe.wait_ge(pads_zeroed, SLOTS)
            for b in range(SLOTS):
                transposes(0, b, first=True)
                gram_products(0, b, first=True)
            pe.wait_ge(weights_loaded, 16 * (KT1 + 1))
            pe.wait_ge(biases_loaded, 48)
            transposes(1, 0)
            gram_products(1, 0)
            layer1(0, first=True)
            transposes(1, 1)
            gram_products(1, 1)
            layers23(0)
            with pe.Fori(2, GROUPS) as q:
                transposes(q, 0)
                gram_products(q, 0)
                layer1(q - 1)
                transposes(q, 1)
                gram_products(q, 1)
                layers23(q - 1)
            layer1(GROUPS - 1)
            layers23(GROUPS - 1)

        @block.vector
        def _(dve):
            for b in range(SLOTS):
                nc.vector.memset(featT[b][:, :, FEATURES:ROWS], 0.0).then_inc(pads_zeroed, 1)

            def copy_features(q, b, first=False):
                if not first:
                    dve.wait_ge(gram_made, CHUNKS * (SLOTS * (q - 1) + b + 1))
                for i in range(T_BATCHES):
                    n = b * T_BATCHES + i
                    dve.wait_ge(transposed, SLOTS * T_BATCHES * q + n + 1)
                    k = min(PER_BANK, FEATURES - i * PER_BANK)
                    if i == 0:
                        nc.vector.tensor_copy(denseT[:, bass.ds(q * GCOLS + b * TILE, TILE)], ps_t[n % 2][:, 0, :])
                    nc.vector.tensor_copy(
                        featT[b][:, :, i * PER_BANK:i * PER_BANK + k].rearrange("d s f -> d f s"),
                        ps_t[n % 2][:, 0:k, :]).then_inc(feat_copied, 1)

            for b in range(SLOTS):
                copy_features(0, b, first=True)
            with dve.Fori(1, GROUPS) as q:
                for b in range(SLOTS):
                    copy_features(q, b)

        @block.scalar
        def _(act):
            with nc.allow_non_contiguous_dma(reason="768 bias values, once"):
                act.dma_start(b1_sb[:, :], b1.rearrange("(m p) -> p m", p=128)).then_inc(biases_loaded, 16)
                act.dma_start(b2_sb[:, :], b2.rearrange("(m p) -> p m", p=128)).then_inc(biases_loaded, 16)
                act.dma_start(w3_sb[:, :], w3.rearrange("(m p) o -> p (m o)", p=128)).then_inc(biases_loaded, 16)

            def copy_gram(q, b, first=False):
                if b == 0 and not first:
                    act.wait_ge(pairs_packed, 16 * len(MOVES) * q)
                for c in range(CHUNKS):
                    n = b * CHUNKS + c
                    act.wait_ge(gram_made, SLOTS * CHUNKS * q + n + 1)
                    cols = gram[:, :, b * TILE + c * CHUNK * PACK:b * TILE + (c + 1) * CHUNK * PACK]
                    cols = cols.rearrange("f g (k s) -> f s k g", s=PACK)
                    for s in range(PACK):
                        last = nc.scalar.activation(
                            cols[:, s, :, :], ps_g[n % 2][s * ROWS:s * ROWS + PAIR_G, :, s * PAIR_G:(s + 1) * PAIR_G],
                            ACT.Copy)
                    last.then_inc(gram_copied, 1)

            def relu1(q):
                for m in range(M1):
                    act.wait_ge(h1_made, M1 * q + m + 1)
                    nc.scalar.activation(h1[:, m, :], ps_m[m % 2][:, 0:GCOLS], ACT.Relu,
                                         bias=b1_sb[:, m:m + 1]).then_inc(h1_copied, 1)

            def relu2(q):
                for m in range(M2):
                    act.wait_ge(h2_made, M2 * q + m + 1)
                    nc.scalar.activation(h2[:, m, :], ps_m[m % 2][:, 0:GCOLS], ACT.Relu,
                                         bias=b2_sb[:, m:m + 1]).then_inc(h2_copied, 1)
                act.wait_ge(y_made, q + 1)
                nc.scalar.activation(y[:, bass.ds(q * SLOTS, SLOTS)], ps_m[0][:, 0:SLOTS], ACT.Copy).then_inc(y_copied, 1)

            for b in range(SLOTS):
                copy_gram(0, b, first=True)
            act.wait_ge(biases_loaded, 48)
            with act.Fori(1, GROUPS) as q:
                copy_gram(q, 0)
                relu1(q - 1)
                copy_gram(q, 1)
                relu2(q - 1)
            relu1(GROUPS - 1)
            relu2(GROUPS - 1)


def kernel(**inputs):
    import numpy as _np
    import concourse.bacc as _bacc
    from concourse import mybir as _mybir
    from concourse.bass_utils import run_bass_kernel_spmd as _run

    nc = _bacc.Bacc("TRN2", target_bir_lowering=False, num_devices=1)
    names = ["r_dense_features", "ids"] + [f"tbl_{f}" for f in range(N_TABLES)]
    names += ["W_top1", "b_top1", "W_top2", "b_top2", "W_top3"]
    arrays, args = {}, {}
    for name in names:
        a = _np.ascontiguousarray(inputs[name])
        arrays[f"in_{name}_dram"] = a
        args[name] = nc.dram_tensor(f"in_{name}_dram", a.shape, _mybir.dt.from_np(a.dtype), kind="ExternalInput").ap()
    out = nc.dram_tensor("out_0_dram", (BATCH, 1), _mybir.dt.float32, kind="ExternalOutput").ap()
    build(nc, args["r_dense_features"], args["ids"], [args[f"tbl_{f}"] for f in range(N_TABLES)], args["W_top1"],
          args["b_top1"], args["W_top2"], args["b_top2"], args["W_top3"], out)
    r = _run(nc, [arrays], core_ids=[0])
    return r.results[0]["out_0_dram"]
```

```python
import concourse.bass as bass
from concourse import mybir
from contextlib import ExitStack

BATCH = 2048
DIM = 128
TABLE_ROWS = [1250, 12500, 1250, 1250, 125000, 1250, 1000, 1000, 1250, 1000, 12500, 12500, 1000,
              1250, 1000, 1000, 1250, 1000, 1000, 1250, 1000, 1000, 12500, 1250, 12500, 12500]
N_TABLES = len(TABLE_ROWS)
FEATURES = N_TABLES + 1
HIDDEN1 = 512
HIDDEN2 = 256

TILE = 128
N_TILES = BATCH // TILE
SLOTS = 2
GROUPS = N_TILES // SLOTS
GCOLS = SLOTS * TILE

N_ONEHOT = 7
SMALL = min(TABLE_ROWS)
ONEHOT_TABLES = [f for f in range(N_TABLES) if TABLE_ROWS[f] == SMALL][:N_ONEHOT]
GATHERED_TABLES = [f for f in range(N_TABLES) if f not in ONEHOT_TABLES]
N_GATHERED = len(GATHERED_TABLES)
TABLE_ORDER = GATHERED_TABLES + ONEHOT_TABLES
SPLIT = N_GATHERED + 1
OH_ROWS = 8
OH_PARTS = SMALL // OH_ROWS
OH_PER_BANK = 512 // GCOLS
OH_BANKS = -(-N_ONEHOT // OH_PER_BANK)

PER_BANK = 512 // TILE
T_BATCHES = -(-SPLIT // PER_BANK)
T_USES = OH_BANKS + SLOTS * T_BATCHES
assert T_USES % 2 == 0

ROWS = 32
PACK = 128 // ROWS
GMM = TILE // PACK
CHUNK = 8
CHUNKS = GMM // CHUNK
PAIR_G = FEATURES - 1

PAIRS = FEATURES * (FEATURES - 1) // 2
PAIR_KT = -(-PAIRS // 128)
KT1 = PAIR_KT + 1
M1 = HIDDEN1 // 128
M2 = HIDDEN2 // 128

UNIT = OH_ROWS * DIM
W1_UNITS = KT1 * HIDDEN1 // UNIT
UNITS = N_ONEHOT + W1_UNITS + M1 * HIDDEN2 // UNIT
STAGES = PAIR_G * GCOLS // UNIT


def pair_moves():
    moves, row = [], 0
    for f in range(FEATURES - 1):
        g = f
        while g < PAIR_G:
            n = min(PAIR_G - g, 128 - row % 128)
            moves.append((f, g, n, row // 128, row % 128))
            g += n
            row += n
    return moves


MOVES = pair_moves()


def w1_rows():
    place = [0] + [f + 1 for f in TABLE_ORDER]
    start = [f * (2 * FEATURES - f - 1) // 2 for f in range(FEATURES)]
    rows = []
    for i in range(FEATURES):
        for j in range(i + 1, FEATURES):
            f, g = sorted((place[i], place[j]))
            rows.append(start[f] + g - f - 1)
    unused = [0] * (PAIR_KT * 128 - PAIRS)
    return rows + unused + list(range(PAIRS, PAIRS + DIM))


def copies_before(n, bank):
    return (n + 1 - bank) // 2


def build(nc, dense, dense_t, ids, tables, w1, b1, w2, b2, w3, out):
    fp32 = mybir.dt.float32
    fp32r = mybir.dt.float32r
    i32 = mybir.dt.int32
    ALU = mybir.AluOpType
    ACT = mybir.ActivationFunctionType

    dense_v = dense.rearrange("(p t) d -> p t d", t=N_TILES)
    ids_v = ids.rearrange("(p t) f -> p (t f)", t=N_TILES)
    out_v = out.rearrange("(p t) o -> p (t o)", t=N_TILES)

    ctx = ExitStack()
    with ctx:
        def sb(name, shape, dt=fp32):
            return ctx.enter_context(nc.sbuf_tensor(name, shape, dt))

        def pb(name, shape):
            return ctx.enter_context(nc.psum_tensor(name, shape, fp32))

        def sem(name):
            return ctx.enter_context(nc.semaphore(name))

        ids_all = sb("ids_all", [128, N_TILES * N_TABLES], i32)
        ids_tile = sb("ids_tile", [128, SLOTS, N_GATHERED], i32)
        ids_cast = sb("ids_cast", [128, SLOTS, N_ONEHOT], fp32r)
        emb = sb("emb", [128, SLOTS, N_GATHERED, DIM])
        dns = sb("dns", [128, SLOTS, DIM])
        featT = sb("featT", [128, SLOTS, TILE, ROWS])
        gram_all = sb("gram", [128, PAIR_G * GCOLS])
        gram = gram_all[0:PAIR_G, :].rearrange("f (g n) -> f g n", g=PAIR_G)
        stage = gram_all[:, 0:STAGES * UNIT].rearrange("p (i n) -> p i n", i=STAGES)
        table_high = sb("table_high", [OH_PARTS, N_ONEHOT, OH_ROWS * DIM], fp32r)
        table_low = sb("table_low", [OH_PARTS, N_ONEHOT, OH_ROWS * DIM], fp32r)
        row_id_int = sb("row_id_int", [128, OH_ROWS], i32)
        row_id = sb("row_id", [128, OH_ROWS])
        onehot = sb("onehot", [128, 2, OH_ROWS, GCOLS], fp32r)
        x1 = sb("x1", [128, KT1, GCOLS])
        x1_high = sb("x1_high", [128, KT1, GCOLS], fp32r)
        x1_low = sb("x1_low", [128, KT1, GCOLS], fp32r)
        h1 = sb("h1", [128, 2, GCOLS])
        h1_high = sb("h1_high", [128, M1, GCOLS], fp32r)
        h1_low = sb("h1_low", [128, M1, GCOLS], fp32r)
        h2 = sb("h2", [128, M2, GCOLS])
        y = sb("y", [128, N_TILES])
        w1_high = sb("w1_high", [128, KT1, HIDDEN1], fp32r)
        w1_low = sb("w1_low", [128, KT1, HIDDEN1], fp32r)
        w2_high = sb("w2_high", [128, M1, HIDDEN2], fp32r)
        w2_low = sb("w2_low", [128, M1, HIDDEN2], fp32r)
        w3_sb = sb("w3_sb", [128, M2])
        b1_sb = sb("b1_sb", [128, M1])
        b2_sb = sb("b2_sb", [128, M2])
        ident = sb("ident", [128, 128])
        ident_r = sb("ident_r", [128, 128], fp32r)

        ps_t = [pb(f"ps_t{i}", [128, PER_BANK * TILE]) for i in range(2)]
        ps_g = [pb(f"ps_g{i}", [128, CHUNK, 128]) for i in range(2)]
        ps_m = [pb(f"ps_m{i}", [128, 512]) for i in range(2)]

        ids_loaded = sem("ids_loaded")
        ids_copied = sem("ids_copied")
        pool_passed = sem("pool_passed")
        sp_passed = sem("sp_passed")
        gathered = [sem(f"gathered{b}") for b in range(SLOTS)]
        dense_loaded = [sem(f"dense_loaded{b}") for b in range(SLOTS)]
        biases_loaded = sem("biases_loaded")
        ident_ready = sem("ident_ready")
        pads_zeroed = sem("pads_zeroed")
        row_ids_made = sem("row_ids_made")
        setup_done = sem("setup_done")
        unit_loaded = [sem(f"unit_loaded{i}") for i in range(UNITS)]
        unit_high = sem("unit_high")
        unit_low = sem("unit_low")
        ids_casted = sem("ids_casted")
        ids_spread = sem("ids_spread")
        onehot_made = sem("onehot_made")
        onehot_used = sem("onehot_used")
        transposed = sem("transposed")
        bank_copied = [sem(f"bank_copied{i}") for i in range(2)]
        gram_made = sem("gram_made")
        gram_copied = sem("gram_copied")
        pairs_packed = sem("pairs_packed")
        dense_packed = sem("dense_packed")
        x1_high_made = sem("x1_high_made")
        x1_low_made = sem("x1_low_made")
        h1_made = sem("h1_made")
        h1_copied = sem("h1_copied")
        h1_low_made = sem("h1_low_made")
        h2_made = sem("h2_made")
        h2_copied = sem("h2_copied")
        y_made = sem("y_made")
        y_copied = sem("y_copied")
        out_stored = sem("out_stored")

        def features(f, n):
            return featT[:, :, :, f:f + n].rearrange("d b s f -> d f b s")

        def transposed_batch(b, i):
            n = OH_BANKS + b * T_BATCHES + i
            k = min(PER_BANK, SPLIT - i * PER_BANK)
            src = ps_t[n % 2][:, 0:k * TILE].rearrange("d (f s) -> d f s", f=k)
            return n, src, features(i * PER_BANK, k)[:, :, b, :]

        x1_tiles = [(128, 0, PAIR_KT - 1), (PAIRS - (PAIR_KT - 1) * 128, PAIR_KT - 1, PAIR_KT), (128, PAIR_KT, KT1)]

        w1_half = KT1 // W1_UNITS

        def unit(u):
            if u < N_ONEHOT:
                src = tables[ONEHOT_TABLES[u]].rearrange("(p k) d -> p k d", k=OH_ROWS)
                return src, table_high[:, u, :], table_low[:, u, :]
            if u < N_ONEHOT + W1_UNITS:
                k = (u - N_ONEHOT) * w1_half
                src = w1.rearrange("(k p) n -> p k n", p=128)[:, k:k + w1_half, :]
                return src, w1_high[:, k:k + w1_half, :], w1_low[:, k:k + w1_half, :]
            return w2.rearrange("(k p) n -> p k n", p=128), w2_high[:, :, :], w2_low[:, :, :]

        def staged(u, like):
            room = stage[0:like.shape[0], u % STAGES, :]
            return room if len(like.shape) == 2 else room.rearrange("p (k n) -> p k n", k=like.shape[1])

        block = ctx.enter_context(nc.Block())

        @block.sync
        def _(sp):
            def load_dense(t, b):
                sp.dma_start(dns[:, b, :], dense_v[:, bass.ds(t, 1), :]).then_inc(dense_loaded[b], 16)

            def pack_x1(q, first=False):
                if not first:
                    sp.wait_ge(x1_high_made, q)
                    sp.sem_inc(sp_passed)
                    sp.wait_ge(x1_low_made, q)
                    sp.sem_inc(sp_passed)
                sp.dma_start(x1[:, PAIR_KT, :], dense_t[:, bass.ds(q * GCOLS, GCOLS)]).then_inc(dense_packed, 16)
                sp.wait_ge(gram_copied, SLOTS * CHUNKS * (q + 1))
                sp.sem_inc(sp_passed)
                for f, g, n, kt, row in MOVES:
                    sp.dma_start(x1[row:row + n, kt, :], gram[f:f + 1, g:g + n, :]).then_inc(pairs_packed, 16)

            def next_dense(q):
                for b in range(SLOTS):
                    sp.wait_ge(transposed, T_BATCHES * (SLOTS * q + b + 1))
                    sp.sem_inc(sp_passed)
                    load_dense(SLOTS * (q + 1) + b, b)

            def load_unit(u):
                src, high, _ = unit(u)
                sp.dma_start(staged(u, src), src).then_inc(unit_loaded[u], 16)

            sp.dma_start(ids_all[:, :], ids_v).then_inc(ids_loaded, 16)
            for b in range(SLOTS):
                load_dense(b, b)
            for u in range(UNITS):
                if u >= STAGES:
                    sp.wait_ge(unit_high, u - STAGES + 1)
                    sp.wait_ge(unit_low, u - STAGES + 1)
                load_unit(u)

            next_dense(0)
            sp.wait_ge(setup_done, 4)
            pack_x1(0, first=True)
            with sp.Fori(1, GROUPS - 1) as q:
                next_dense(q)
                pack_x1(q)
            pack_x1(GROUPS - 1)
            sp.wait_ge(y_copied, GROUPS)
            sp.dma_start(out_v, y[:, :]).then_inc(out_stored, 16)
            sp.wait_ge(out_stored, 16)

        @block.gpsimd
        def _(pool):
            pool.memset(ident[:, :], 0.0).then_inc(ident_ready, 1)
            pool.wait_ge(ident_ready, 1)
            pool.affine_select(out=ident[:, :], in_=ident[:, :], compare_op=ALU.not_equal, fill=1.0,
                               base=0, pattern=[[-1, 128]], channel_multiplier=1).then_inc(ident_ready, 1)

            pool.iota(row_id_int[:, :], pattern=[[1, OH_ROWS]], base=0, channel_multiplier=OH_ROWS).then_inc(row_ids_made, 1)

            def gather(q, b, first=False):
                t = SLOTS * q + b
                if not first:
                    pool.wait_ge(transposed, T_BATCHES * (t - SLOTS + 1))
                    pool.sem_inc(pool_passed)
                pool.tensor_copy(ids_tile[:, b, :], ids_all[:, bass.ds(t * N_TABLES, N_GATHERED)]).then_inc(ids_copied, 1)
                pool.wait_ge(ids_copied, t + 1)
                pool.sem_inc(pool_passed)
                for f in range(N_GATHERED):
                    pool.indirect_dma_start(
                        out=emb[:, b, f, :], out_offset=None, in_=tables[GATHERED_TABLES[f]][:, :],
                        in_offset=bass.IndirectOffsetOnAxis(ap=ids_tile[:, b, f:f + 1], axis=0),
                    ).then_inc(gathered[b], 16)

            pool.wait_ge(ids_loaded, 16)
            for b in range(SLOTS):
                gather(0, b, first=True)
            with pool.Fori(1, GROUPS) as q:
                for b in range(SLOTS):
                    gather(q, b)

        @block.tensor
        def _(pe):
            def spread_ids(i):
                for b in range(SLOTS):
                    last = nc.tensor.matmul(ps_m[i % 2][:, b * TILE:(b + 1) * TILE],
                                            ids_cast[:, b, i:i + 1].to_broadcast([128, 128]), ident_r[:, :],
                                            start=True, stop=True)
                last.then_inc(ids_spread, 1)

            def spread_first_ids(q):
                pe.wait_ge(ids_casted, q + 1)
                for i in range(2):
                    spread_ids(i)

            def bank_free(q, n):
                pe.wait_ge(bank_copied[n % 2], T_USES // 2 * q + n // 2)

            def onehot_products(q, first=False):
                for i in range(N_ONEHOT):
                    j, k = i // OH_PER_BANK, i % OH_PER_BANK
                    pe.wait_ge(onehot_made, N_ONEHOT * q + i + 1)
                    if first:
                        pe.wait_ge(unit_high, i + 1)
                        pe.wait_ge(unit_low, i + 1)
                    if k == 0 and not (first and j < 2):
                        bank_free(q, j)
                    for r in range(OH_ROWS):
                        for part in (table_high, table_low):
                            last = nc.tensor.matmul(
                                ps_t[j % 2][:, k * GCOLS:(k + 1) * GCOLS], part[:, i, r * DIM:(r + 1) * DIM],
                                onehot[0:OH_PARTS, i % 2, r, :], start=(r == 0 and part is table_high),
                                stop=(r == OH_ROWS - 1 and part is table_low))
                    last.then_inc(onehot_used, 1)
                    if i + 2 < N_ONEHOT:
                        spread_ids(i + 2)

            def transposes(q, b):
                pe.wait_ge(gathered[b], 16 * N_GATHERED * (q + 1))
                pe.wait_ge(dense_loaded[b], 16 * (q + 1))
                for i in range(T_BATCHES):
                    n = OH_BANKS + b * T_BATCHES + i
                    bank_free(q, n)
                    for k in range(min(PER_BANK, SPLIT - i * PER_BANK)):
                        f = i * PER_BANK + k
                        src = dns[:, b, :] if f == 0 else emb[:, b, f - 1, :]
                        last = nc.tensor.transpose(ps_t[n % 2][:, k * TILE:(k + 1) * TILE], src, ident[:, :])
                    last.then_inc(transposed, 1)

            def features_ready(q, b):
                for bank in range(2):
                    n = copies_before(OH_BANKS + T_BATCHES * (b + 1), bank)
                    pe.wait_ge(bank_copied[bank], T_USES // 2 * q + n)

            def gram_chunk(q, b, c, first=False):
                n = b * CHUNKS + c
                if not (first and n < 2):
                    pe.wait_ge(gram_copied, SLOTS * CHUNKS * q + n - 1)
                for k in range(CHUNK):
                    s = (c * CHUNK + k) * PACK
                    last = nc.tensor.matmul(ps_g[n % 2][:, k, 0:PACK * PAIR_G], featT[:, b, s:s + PACK, :],
                                            featT[:, b, s:s + PACK, 1:FEATURES], start=True, stop=True)
                last.then_inc(gram_made, 1)

            def split_products(out, w_high, w_low, x_high, x_low, first, final):
                nc.tensor.matmul(out, w_high, x_high, start=first, stop=False)
                nc.tensor.matmul(out, w_high, x_low, start=False, stop=False)
                return nc.tensor.matmul(out, w_low, x_high, start=False, stop=final)

            def layer1(q):
                pe.wait_ge(x1_high_made, q + 1)
                pe.wait_ge(x1_low_made, q + 1)
                for m in range(M1):
                    if m >= 2:
                        pe.wait_ge(h1_copied, M1 * q + m - 1)
                    for kt in range(KT1):
                        n = min(128, PAIRS - kt * 128) if kt < PAIR_KT else 128
                        cols = slice(m * 128, (m + 1) * 128)
                        last = split_products(ps_m[m % 2][:, 0:GCOLS], w1_high[0:n, kt, cols], w1_low[0:n, kt, cols],
                                              x1_high[0:n, kt, :], x1_low[0:n, kt, :], kt == 0, kt == KT1 - 1)
                    last.then_inc(h1_made, 1)

            def layer2(q):
                pe.wait_ge(h1_copied, M1 * (q + 1))
                pe.wait_ge(h1_low_made, M1 * (q + 1))
                for m in range(M2):
                    for kt in range(M1):
                        cols = slice(m * 128, (m + 1) * 128)
                        last = split_products(ps_m[m % 2][:, 0:GCOLS], w2_high[:, kt, cols], w2_low[:, kt, cols],
                                              h1_high[:, kt, :], h1_low[:, kt, :], kt == 0, kt == M1 - 1)
                    last.then_inc(h2_made, 1)

            def layer3(q):
                pe.wait_ge(h2_copied, M2 * (q + 1))
                for b in range(SLOTS):
                    for kt in range(M2):
                        last = nc.tensor.matmul(ps_t[0][:, b:b + 1], h2[:, kt, b * TILE:(b + 1) * TILE],
                                                w3_sb[:, kt:kt + 1], start=(kt == 0), stop=(kt == M2 - 1))
                last.then_inc(y_made, 1)

            pe.wait_ge(ident_ready, 2)
            pe.wait_ge(setup_done, 3)
            spread_first_ids(0)
            onehot_products(0, first=True)
            transposes(0, 0)
            features_ready(0, 0)
            for c in range(CHUNKS):
                gram_chunk(0, 0, c, first=True)
            transposes(0, 1)
            features_ready(0, 1)
            gram_chunk(0, 1, 0)
            spread_first_ids(1)
            for c in range(1, CHUNKS):
                gram_chunk(0, 1, c)
            pe.wait_ge(unit_high, UNITS)
            pe.wait_ge(unit_low, UNITS)
            with pe.Fori(1, GROUPS - 1) as q:
                onehot_products(q)
                transposes(q, 0)
                features_ready(q, 0)
                for c in range(CHUNKS):
                    gram_chunk(q, 0, c)
                layer1(q - 1)
                transposes(q, 1)
                layer2(q - 1)
                features_ready(q, 1)
                gram_chunk(q, 1, 0)
                layer3(q - 1)
                spread_first_ids(q + 1)
                for c in range(1, CHUNKS):
                    gram_chunk(q, 1, c)
                pe.wait_ge(y_copied, q)
            q = GROUPS - 1
            onehot_products(q)
            transposes(q, 0)
            features_ready(q, 0)
            for c in range(CHUNKS):
                gram_chunk(q, 0, c)
            layer1(q - 1)
            transposes(q, 1)
            layer2(q - 1)
            features_ready(q, 1)
            gram_chunk(q, 1, 0)
            layer3(q - 1)
            for c in range(1, CHUNKS):
                gram_chunk(q, 1, c)
            layer1(q)
            layer2(q)
            pe.wait_ge(y_copied, q)
            layer3(q)

        @block.vector
        def _(dve):
            def cast_ids(q):
                src = ids_all[:, bass.ds(q * SLOTS * N_TABLES, SLOTS * N_TABLES)].rearrange("p (b f) -> p b f", b=SLOTS)
                nc.vector.tensor_copy(ids_cast[:, :, :], src[:, :, N_GATHERED:N_TABLES]).then_inc(ids_casted, 1)

            def make_onehot(q, i):
                dve.wait_ge(ids_spread, N_ONEHOT * q + i + 1)
                if i >= 2:
                    dve.wait_ge(onehot_used, N_ONEHOT * q + i - 1)
                elif not (isinstance(q, int) and q == 0):
                    dve.wait_ge(onehot_used, N_ONEHOT * (q - 1) + (N_ONEHOT - 1 - i) // 2 * 2 + i + 1)
                nc.vector.tensor_tensor(
                    onehot[:, i % 2, :, :], ps_m[i % 2][:, 0:GCOLS].unsqueeze(1).to_broadcast([128, OH_ROWS, GCOLS]),
                    row_id[:, :].unsqueeze(2).to_broadcast([128, OH_ROWS, GCOLS]), ALU.is_equal).then_inc(onehot_made, 1)

            def copy_transposes(q, b, i):
                n, src, dst = transposed_batch(b, i)
                if n % 2 == 0:
                    dve.wait_ge(transposed, SLOTS * T_BATCHES * q + b * T_BATCHES + i + 1)
                    nc.vector.tensor_copy(dst, src).then_inc(bank_copied[0], 1)

            def split_x1(q):
                dve.wait_ge(x1_high_made, q + 1)
                for p, k0, k1 in x1_tiles:
                    last = nc.vector.tensor_sub(x1_low[0:p, k0:k1, :], x1[0:p, k0:k1, :],
                                                x1_high[0:p, k0:k1, :].bitcast(fp32))
                last.then_inc(x1_low_made, 1)

            def split_h1(q, m):
                dve.wait_ge(h1_copied, M1 * q + m + 1)
                nc.vector.tensor_sub(h1_low[:, m, :], h1[:, m % 2, :],
                                     h1_high[:, m, :].bitcast(fp32)).then_inc(h1_low_made, 1)

            def group(q, mlp=True, following=True):
                for i in range(2, N_ONEHOT):
                    make_onehot(q, i)
                if following:
                    cast_ids(q + 1)
                for i in range(T_BATCHES):
                    copy_transposes(q, 0, i)
                if mlp:
                    split_x1(q - 1)
                    for m in range(M1 - 1):
                        split_h1(q - 1, m)
                for i in range(T_BATCHES):
                    copy_transposes(q, 1, i)
                    if i == 1 and mlp:
                        split_h1(q - 1, M1 - 1)
                if following:
                    for i in range(2):
                        make_onehot(q + 1, i)

            nc.vector.memset(featT[:, :, :, FEATURES:ROWS], 0.0).then_inc(setup_done, 1)
            dve.wait_ge(row_ids_made, 1)
            nc.vector.tensor_copy(row_id[:, :], row_id_int[:, :]).then_inc(setup_done, 1)
            dve.wait_ge(ident_ready, 2)
            nc.vector.tensor_copy(ident_r[:, :], ident[:, :]).then_inc(setup_done, 1)
            nc.vector.memset(x1[:, PAIR_KT - 1, :], 0.0).then_inc(setup_done, 1)
            dve.wait_ge(ids_loaded, 16)
            dve.wait_ge(setup_done, 4)
            cast_ids(0)
            for i in range(2):
                make_onehot(0, i)
            for u in range(UNITS):
                dve.wait_ge(unit_high, u + 1)
                _, high, low = unit(u)
                nc.vector.tensor_sub(low, staged(u, low), high.bitcast(fp32)).then_inc(unit_low, 1)
            group(0, mlp=False)
            with dve.Fori(1, GROUPS - 1) as q:
                group(q)
            group(GROUPS - 1, following=False)
            split_x1(GROUPS - 1)
            for m in range(M1):
                split_h1(GROUPS - 1, m)

        @block.scalar
        def _(act):
            with nc.allow_non_contiguous_dma(reason="768 bias values, once"):
                act.dma_start(b1_sb[:, :], b1.rearrange("(m p) -> p m", p=128)).then_inc(biases_loaded, 16)
                act.dma_start(b2_sb[:, :], b2.rearrange("(m p) -> p m", p=128)).then_inc(biases_loaded, 16)
                act.dma_start(w3_sb[:, :], w3.rearrange("(m p) o -> p (m o)", p=128)).then_inc(biases_loaded, 16)

            for u in range(UNITS):
                act.wait_ge(unit_loaded[u], 16)
                _, high, _ = unit(u)
                nc.scalar.activation(high, staged(u, high), ACT.Copy).then_inc(unit_high, 1)

            def copy_products(q):
                for j in range(OH_BANKS):
                    k = min(OH_PER_BANK, N_ONEHOT - OH_PER_BANK * j)
                    act.wait_ge(onehot_used, N_ONEHOT * q + OH_PER_BANK * j + k)
                    nc.scalar.activation(
                        features(SPLIT + OH_PER_BANK * j, k),
                        ps_t[j % 2][:, 0:k * GCOLS].rearrange("d (f b s) -> d f b s", f=k, b=SLOTS),
                        ACT.Copy).then_inc(bank_copied[j % 2], 1)

            def copy_transposes(q, b):
                for i in range(T_BATCHES):
                    n, src, dst = transposed_batch(b, i)
                    if n % 2 == 1:
                        act.wait_ge(transposed, SLOTS * T_BATCHES * q + b * T_BATCHES + i + 1)
                        nc.scalar.activation(dst, src, ACT.Copy).then_inc(bank_copied[1], 1)

            def copy_gram(q, b, c):
                n = b * CHUNKS + c
                act.wait_ge(gram_made, SLOTS * CHUNKS * q + n + 1)
                cols = gram[:, :, b * TILE + c * CHUNK * PACK:b * TILE + (c + 1) * CHUNK * PACK]
                cols = cols.rearrange("f g (k s) -> f s k g", s=PACK)
                for s in range(PACK):
                    last = nc.scalar.activation(
                        cols[:, s, :, :], ps_g[n % 2][s * ROWS:s * ROWS + PAIR_G, :, s * PAIR_G:(s + 1) * PAIR_G],
                        ACT.Copy)
                last.then_inc(gram_copied, 1)

            def split_x1(q):
                act.wait_ge(dense_packed, 16 * (q + 1))
                act.wait_ge(pairs_packed, 16 * len(MOVES) * (q + 1))
                for p, k0, k1 in x1_tiles:
                    last = nc.scalar.activation(x1_high[0:p, k0:k1, :], x1[0:p, k0:k1, :], ACT.Copy)
                last.then_inc(x1_high_made, 1)

            def relu1(q, first=False):
                for m in range(M1):
                    act.wait_ge(h1_made, M1 * q + m + 1)
                    if not (first and m < 2):
                        act.wait_ge(h1_low_made, M1 * q + m - 1)
                    nc.scalar.activation(h1[:, m % 2, :], ps_m[m % 2][:, 0:GCOLS], ACT.Relu, bias=b1_sb[:, m:m + 1])
                    nc.scalar.activation(h1_high[:, m, :], ps_m[m % 2][:, 0:GCOLS], ACT.Relu,
                                         bias=b1_sb[:, m:m + 1]).then_inc(h1_copied, 1)

            def relu2(q):
                for m in range(M2):
                    act.wait_ge(h2_made, M2 * q + m + 1)
                    nc.scalar.activation(h2[:, m, :], ps_m[m % 2][:, 0:GCOLS], ACT.Relu,
                                         bias=b2_sb[:, m:m + 1]).then_inc(h2_copied, 1)

            def copy_scores(q):
                act.wait_ge(y_made, q + 1)
                nc.scalar.activation(y[:, bass.ds(q * SLOTS, SLOTS)], ps_t[0][:, 0:SLOTS], ACT.Copy).then_inc(y_copied, 1)

            def group(q, mlp=True, first_mlp=False):
                copy_products(q)
                copy_transposes(q, 0)
                for c in range(CHUNKS):
                    if mlp and c == 0:
                        split_x1(q - 1)
                    copy_gram(q, 0, c)
                if mlp:
                    relu1(q - 1, first=first_mlp)
                copy_transposes(q, 1)
                if mlp:
                    relu2(q - 1)
                copy_gram(q, 1, 0)
                if mlp:
                    copy_scores(q - 1)
                for c in range(1, CHUNKS):
                    copy_gram(q, 1, c)

            act.wait_ge(unit_low, UNITS)
            group(0, mlp=False)
            act.wait_ge(biases_loaded, 48)
            group(1, first_mlp=True)
            with act.Fori(2, GROUPS) as q:
                group(q)
            split_x1(GROUPS - 1)
            relu1(GROUPS - 1)
            relu2(GROUPS - 1)
            copy_scores(GROUPS - 1)


def kernel(**inputs):
    import numpy as _np
    import concourse.bacc as _bacc
    from concourse import mybir as _mybir
    from concourse.bass_utils import run_bass_kernel_spmd as _run

    nc = _bacc.Bacc("TRN2", target_bir_lowering=False, num_devices=1)
    by_tile = _np.asarray(inputs["r_dense_features"]).reshape(TILE, N_TILES, DIM).transpose(2, 1, 0)
    inputs["dense_t"] = by_tile.reshape(DIM, BATCH)
    names = ["r_dense_features", "dense_t", "ids"] + [f"tbl_{f}" for f in range(N_TABLES)]
    names += ["W_top1", "b_top1", "W_top2", "b_top2", "W_top3"]
    arrays, args = {}, {}
    for name in names:
        a = inputs[name]
        if name == "ids":
            a = a[:, TABLE_ORDER]
        if name == "W_top1":
            a = a[w1_rows()]
        a = _np.ascontiguousarray(a)
        arrays[f"in_{name}_dram"] = a
        args[name] = nc.dram_tensor(f"in_{name}_dram", a.shape, _mybir.dt.from_np(a.dtype), kind="ExternalInput").ap()
    out = nc.dram_tensor("out_0_dram", (BATCH, 1), _mybir.dt.float32, kind="ExternalOutput").ap()
    build(nc, args["r_dense_features"], args["dense_t"], args["ids"], [args[f"tbl_{f}"] for f in range(N_TABLES)], args["W_top1"],
          args["b_top1"], args["W_top2"], args["b_top2"], args["W_top3"], out)
    r = _run(nc, [arrays], core_ids=[0])
    return r.results[0]["out_0_dram"]
```

```python
import concourse.bass as bass
from concourse import mybir
from contextlib import ExitStack

BATCH = 2048
DIM = 128
TABLE_ROWS = [1250, 12500, 1250, 1250, 125000, 1250, 1000, 1000, 1250, 1000, 12500, 12500, 1000,
              1250, 1000, 1000, 1250, 1000, 1000, 1250, 1000, 1000, 12500, 1250, 12500, 12500]
N_TABLES = len(TABLE_ROWS)
FEATURES = N_TABLES + 1
HIDDEN1 = 512
HIDDEN2 = 256

TILE = 128
N_TILES = BATCH // TILE
SLOTS = 2
GROUPS = N_TILES // SLOTS
GCOLS = SLOTS * TILE

N_ONEHOT = 7
N_EXTRA = 2
SMALL = min(TABLE_ROWS)
SMALL_TABLES = [f for f in range(N_TABLES) if TABLE_ROWS[f] == SMALL]
ONEHOT_TABLES, EXTRA_TABLES = SMALL_TABLES[:N_ONEHOT], SMALL_TABLES[N_ONEHOT:N_ONEHOT + N_EXTRA]
GATHERED_TABLES = [f for f in range(N_TABLES) if f not in ONEHOT_TABLES + EXTRA_TABLES] + EXTRA_TABLES
N_GATHERED = len(GATHERED_TABLES)
TABLE_ORDER = GATHERED_TABLES + ONEHOT_TABLES
SPLIT = N_GATHERED + 1
OH_ROWS = 8
OH_PARTS = SMALL // OH_ROWS
OH_PER_BANK = 512 // GCOLS
ONEHOT_BUFS = 3

PER_BANK = 512 // TILE
T_BATCHES = -(-N_GATHERED // PER_BANK)
assert T_BATCHES == -(-(N_GATHERED - N_EXTRA) // PER_BANK)
BANK_BATCHES = [(T_BATCHES + 1) // 2, T_BATCHES // 2]

ROWS = 32
PACK = 128 // ROWS
GMM = TILE // PACK
CHUNK = 8
CHUNKS = GMM // CHUNK
PAIR_G = FEATURES - 1

PAIRS = FEATURES * (FEATURES - 1) // 2
PAIR_KT = -(-PAIRS // 128)
PAIR_ROWS = PAIRS // PAIR_KT
BLOCK_KT = -(-PAIR_G // PACK)
KT1 = PAIR_KT + 1
M1 = HIDDEN1 // 128
M2 = HIDDEN2 // 128

UNIT = OH_ROWS * DIM
W1_UNITS = KT1 * HIDDEN1 // UNIT
UNITS = N_EXTRA + N_ONEHOT + W1_UNITS + M1 * HIDDEN2 // UNIT
STAGES = PAIR_G * GCOLS // UNIT


def pair_moves():
    moves, left = [], list(range(PAIR_G))
    for kt in range(PAIR_KT):
        row = 0
        for f in list(left):
            if row + PAIR_G - f <= PAIR_ROWS:
                moves.append((f, kt, row))
                row += PAIR_G - f
                left.remove(f)
        assert row == PAIR_ROWS
    return moves


MOVES = pair_moves()
EARLY_MOVES = 18


def w1_rows():
    unused = [0] * (128 - PAIR_ROWS)
    rows = []
    for kt in range(PAIR_KT):
        for f, tile, _ in MOVES:
            if tile == kt:
                rows += [pair_row(f, g) for g in range(f, PAIR_G)]
        rows += unused
    return rows + list(range(PAIRS, PAIRS + DIM))


def extra(q):
    return N_EXTRA if isinstance(q, int) and q == 0 else 0


def products_before(q):
    return 0 if isinstance(q, int) and q == 0 else N_ONEHOT * q + N_EXTRA


def product_banks(q):
    return -(-(N_ONEHOT + extra(q)) // OH_PER_BANK)


def product_banks_before(q):
    return 0 if isinstance(q, int) and q == 0 else product_banks(1) * (q - 1) + product_banks(0)


def batches_after(q, i):
    return [k for k in range(T_BATCHES) if max(0, N_ONEHOT + extra(q) - 1 - T_BATCHES + k) == i]


def pair_row(f, g):
    place = [0] + [t + 1 for t in TABLE_ORDER]
    i, j = sorted((place[f], place[g + 1]))
    return i * (2 * FEATURES - i - 1) // 2 + j - i - 1


def build(nc, dense_t, ids, tables, w1, w1_blocks, b1, w2, b2, w3, out):
    fp32 = mybir.dt.float32
    fp32r = mybir.dt.float32r
    i32 = mybir.dt.int32
    ALU = mybir.AluOpType
    ACT = mybir.ActivationFunctionType

    ids_v = ids.rearrange("(p t) f -> p (t f)", t=N_TILES)
    out_v = out.rearrange("(p t) o -> p (t o)", t=N_TILES)

    ctx = ExitStack()
    with ctx:
        def sb(name, shape, dt=fp32):
            return ctx.enter_context(nc.sbuf_tensor(name, shape, dt))

        def pb(name, shape):
            return ctx.enter_context(nc.psum_tensor(name, shape, fp32))

        def sem(name):
            return ctx.enter_context(nc.semaphore(name))

        ids_all = sb("ids_all", [128, N_TILES * N_TABLES], i32)
        ids_tile = sb("ids_tile", [128, SLOTS, N_GATHERED], i32)
        ids_cast = sb("ids_cast", [128, SLOTS, N_EXTRA + N_ONEHOT], fp32r)
        emb = sb("emb", [128, SLOTS, N_GATHERED, DIM])
        featT = sb("featT", [128, SLOTS, TILE, ROWS])
        gram_all = sb("gram", [128, PAIR_G * GCOLS])
        gram = gram_all[0:PAIR_G, :].rearrange("f (g n) -> f g n", g=PAIR_G)
        stage = gram_all[:, 0:STAGES * UNIT].rearrange("p (i n) -> p i n", i=STAGES)
        table_high = sb("table_high", [OH_PARTS, N_ONEHOT, OH_ROWS * DIM], fp32r)
        table_low = sb("table_low", [OH_PARTS, N_ONEHOT, OH_ROWS * DIM], fp32r)
        row_id_int = sb("row_id_int", [128, OH_ROWS], i32)
        row_id = sb("row_id", [128, OH_ROWS])
        x1 = sb("x1", [128, KT1, GCOLS])
        x1_high = sb("x1_high", [128, KT1, GCOLS], fp32r)
        x1_low = sb("x1_low", [128, KT1, GCOLS], fp32r)
        h1 = sb("h1", [128, 2, GCOLS])
        h2 = h1
        h1_high = sb("h1_high", [128, M1, GCOLS], fp32r)
        h1_low = sb("h1_low", [128, M1, GCOLS], fp32r)
        y = sb("y", [128, N_TILES])
        w1_high = sb("w1_high", [128, KT1, HIDDEN1], fp32r)
        w1_low = sb("w1_low", [128, KT1, HIDDEN1], fp32r)
        w2_high = sb("w2_high", [128, M1, HIDDEN2], fp32r)
        w2_low = sb("w2_low", [128, M1, HIDDEN2], fp32r)
        w3_sb = sb("w3_sb", [128, M2])
        b1_sb = sb("b1_sb", [128, M1])
        b2_sb = sb("b2_sb", [128, M2])
        ident = sb("ident", [128, 128])
        ident_r = sb("ident_r", [128, 128], fp32r)
        with nc.sbuf_tensor("onehot", [128, ONEHOT_BUFS, OH_ROWS, GCOLS], fp32r) as onehot:
            pass
        w1_quads = sb("w1_quads", [128, BLOCK_KT, HIDDEN1])
        blocks = emb[:, 0, 0:BLOCK_KT * SLOTS, :].rearrange("p (k b) n -> p k (b n)", b=SLOTS)

        ps_t = [pb(f"ps_t{i}", [128, PER_BANK * TILE]) for i in range(2)]
        ps_g = [pb(f"ps_g{i}", [128, CHUNK, 128]) for i in range(2)]
        ps_y = ps_t[T_BATCHES % 2]
        ps_m = [pb(f"ps_m{i}", [128, 512]) for i in range(2)]

        ids_loaded = sem("ids_loaded")
        ids_copied = sem("ids_copied")
        pool_passed = sem("pool_passed")
        sp_passed = sem("sp_passed")
        gathered = [sem(f"gathered{b}") for b in range(SLOTS)]
        dense_loaded = sem("dense_loaded")
        dense_copied = sem("dense_copied")
        dense_high = sem("dense_high")
        dense_low = sem("dense_low")
        biases_loaded = sem("biases_loaded")
        ident_ready = sem("ident_ready")
        row_ids_made = sem("row_ids_made")
        setup_done = sem("setup_done")
        unit_loaded = [sem(f"unit_loaded{i}") for i in range(UNITS)]
        unit_high = sem("unit_high")
        unit_low = sem("unit_low")
        ids_casted = sem("ids_casted")
        ids_spread = sem("ids_spread")
        onehot_made = sem("onehot_made")
        onehot_used = sem("onehot_used")
        transposed = sem("transposed")
        bank_copied = [sem(f"bank_copied{i}") for i in range(2)]
        products_copied = sem("products_copied")
        gram_made = sem("gram_made")
        gram_copied = sem("gram_copied")
        blocks_copied = sem("blocks_copied")
        blocks_weights_loaded = sem("blocks_weights_loaded")
        x1_packed = [sem(f"x1_packed{b}") for b in range(SLOTS)]
        both_packed = sem("both_packed")
        x1_high_made = sem("x1_high_made")
        x1_low_made = sem("x1_low_made")
        h1_made = sem("h1_made")
        h1_copied = sem("h1_copied")
        h1_low_made = sem("h1_low_made")
        h2_made = sem("h2_made")
        h2_copied = sem("h2_copied")
        y_made = sem("y_made")
        y_copied = sem("y_copied")
        out_stored = sem("out_stored")

        def features(f, n):
            return featT[:, :, :, f:f + n].rearrange("d b s f -> d f b s")

        def onehot_rows(i, n):
            per_buffer = CHUNK * 128 // GCOLS
            at = i % per_buffer * GCOLS
            return ps_g[i // per_buffer % 2][:, :, :].rearrange("p k n -> p (k n)")[:, at:at + n * GCOLS]

        def transposed_batch(q, b, i):
            bank = i % 2
            k = min(PER_BANK, N_GATHERED - extra(q) - i * PER_BANK)
            src = ps_t[bank][:, 0:k * TILE].rearrange("d (f s) -> d f s", f=k)
            return bank, src, features(1 + i * PER_BANK, k)[:, :, b, :]

        def pairs_of(b):
            return slice(0, PAIR_ROWS), slice(0, PAIR_KT), slice(b * TILE, (b + 1) * TILE)

        w1_half = KT1 // W1_UNITS

        def table_parts(n):
            if n >= N_EXTRA:
                return table_high[:, n - N_EXTRA, :], table_low[:, n - N_EXTRA, :]
            room = ((x1_high, x1_low), (h1_high, h1_low))[n]
            return tuple(part[0:OH_PARTS, :, :].rearrange("p k n -> p (k n)") for part in room)

        def unit(u):
            if u < N_EXTRA + N_ONEHOT:
                src = tables[(EXTRA_TABLES + ONEHOT_TABLES)[u]].rearrange("(p k) d -> p k d", k=OH_ROWS)
                return (src,) + table_parts(u)
            if u < UNITS - 1:
                k = (u - N_EXTRA - N_ONEHOT) * w1_half
                src = w1.rearrange("(k p) n -> p k n", p=128)[:, k:k + w1_half, :]
                return src, w1_high[:, k:k + w1_half, :], w1_low[:, k:k + w1_half, :]
            return w2.rearrange("(k p) n -> p k n", p=128), w2_high[:, :, :], w2_low[:, :, :]

        def staged(u, like):
            room = stage[0:like.shape[0], u % STAGES, :]
            return room if len(like.shape) == 2 else room.rearrange("p (k n) -> p k n", k=like.shape[1])

        def block_move(n, s, j):
            k = len(range(j, PAIR_G, PACK))
            buf = ps_g[n % 2][s * ROWS:(s + 1) * ROWS, :, s * PAIR_G + j:s * PAIR_G + j + (k - 1) * PACK + 1:PACK]
            first = n * CHUNK * PACK + s
            dst = blocks[j * ROWS:(j + 1) * ROWS, 0:k, first:first + (CHUNK - 1) * PACK + 1:PACK]
            return dst, buf.rearrange("f m k -> f k m")

        block = ctx.enter_context(nc.Block())

        @block.sync
        def _(sp):
            def load_dense(q, first=False):
                if not first:
                    sp.wait_ge(dense_copied, q)
                    sp.sem_inc(sp_passed)
                    sp.wait_ge(dense_high, q)
                    sp.sem_inc(sp_passed)
                    sp.wait_ge(dense_low, q)
                    sp.sem_inc(sp_passed)
                sp.dma_start(x1[:, PAIR_KT, :], dense_t[:, bass.ds(q * GCOLS, GCOLS)]).then_inc(dense_loaded, 16)

            def gram_ready(q, b):
                sp.wait_ge(gram_copied, CHUNKS * (SLOTS * q + b + 1))
                sp.sem_inc(sp_passed)

            def move_pairs(moves, cols, moved):
                for f, kt, row in moves:
                    sp.dma_start(x1[row:row + PAIR_G - f, kt, cols], gram[f:f + 1, f:PAIR_G, cols]).then_inc(moved, 16)

            def pack_x1(q, b):
                sp.wait_ge(x1_high_made, SLOTS * (q - 1) + b + 1)
                sp.sem_inc(sp_passed)
                sp.wait_ge(x1_low_made, SLOTS * (q - 1) + b + 1)
                sp.sem_inc(sp_passed)
                gram_ready(q, b)
                move_pairs(MOVES, slice(b * TILE, (b + 1) * TILE), x1_packed[b])

            def pack_first_x1():
                gram_ready(0, 0)
                move_pairs(MOVES[:EARLY_MOVES], slice(0, TILE), x1_packed[0])
                load_dense(1)
                gram_ready(0, 1)
                move_pairs(MOVES[EARLY_MOVES:], slice(0, GCOLS), both_packed)
                move_pairs(MOVES[:EARLY_MOVES], slice(TILE, GCOLS), x1_packed[1])

            def load_unit(u):
                src, high, _ = unit(u)
                sp.dma_start(staged(u, src), src).then_inc(unit_loaded[u], 16)

            sp.dma_start(ids_all[:, :], ids_v).then_inc(ids_loaded, 16)
            load_dense(0, first=True)
            for u in range(UNITS):
                if u >= STAGES:
                    sp.wait_ge(unit_high, u - STAGES + 1)
                    sp.wait_ge(unit_low, u - STAGES + 1)
                load_unit(u)

            pack_first_x1()
            with sp.Fori(1, GROUPS - 1) as q:
                pack_x1(q, 0)
                load_dense(q + 1)
                pack_x1(q, 1)
            sp.wait_ge(y_copied, GROUPS)
            sp.dma_start(out_v, y[:, :]).then_inc(out_stored, 16)
            sp.wait_ge(out_stored, 16)

        @block.gpsimd
        def _(pool):
            pool.memset(ident[:, :], 0.0).then_inc(ident_ready, 1)
            pool.wait_ge(ident_ready, 1)
            pool.affine_select(out=ident[:, :], in_=ident[:, :], compare_op=ALU.not_equal, fill=1.0,
                               base=0, pattern=[[-1, 128]], channel_multiplier=1).then_inc(ident_ready, 1)

            pool.iota(row_id_int[:, :], pattern=[[1, OH_ROWS]], base=0, channel_multiplier=OH_ROWS)\
                .then_inc(row_ids_made, 1)

            def gather(q, b, first=False):
                t = SLOTS * q + b
                if not first:
                    pool.wait_ge(transposed, T_BATCHES * (t - SLOTS + 1))
                    pool.sem_inc(pool_passed)
                pool.tensor_copy(ids_tile[:, b, :], ids_all[:, bass.ds(t * N_TABLES, N_GATHERED)])\
                    .then_inc(ids_copied, 1)
                pool.wait_ge(ids_copied, t + 1)
                pool.sem_inc(pool_passed)
                for f in range(N_GATHERED - extra(q)):
                    pool.indirect_dma_start(
                        out=emb[:, b, f, :], out_offset=None, in_=tables[GATHERED_TABLES[f]][:, :],
                        in_offset=bass.IndirectOffsetOnAxis(ap=ids_tile[:, b, f:f + 1], axis=0),
                    ).then_inc(gathered[b], 16)

            pool.wait_ge(ids_loaded, 16)
            for b in range(SLOTS):
                gather(0, b, first=True)
            with pool.Fori(1, GROUPS) as q:
                for b in range(SLOTS):
                    gather(q, b)

        @block.tensor
        def _(pe):
            def spread_ids(q, i):
                n = N_EXTRA - extra(q) + i
                for b in range(SLOTS):
                    last = nc.tensor.matmul(ps_m[i % 2][:, b * TILE:(b + 1) * TILE],
                                            ids_cast[:, b, n:n + 1].to_broadcast([128, 128]), ident_r[:, :],
                                            start=True, stop=True)
                last.then_inc(ids_spread, 1)

            def spread_third_ids(q):
                pe.wait_ge(onehot_made, products_before(q) + 1)
                spread_ids(q, 2)

            def onehot_product(q, i, first=False):
                pe.wait_ge(onehot_made, products_before(q) + i + 1)
                if first:
                    pe.wait_ge(unit_high, i + 1)
                    pe.wait_ge(unit_low, i + 1)
                    if i >= 2 * CHUNK * 128 // GCOLS:
                        pe.wait_ge(products_copied, (i - 2 * CHUNK * 128 // GCOLS) // OH_PER_BANK + 1)
                elif i in (0, CHUNK * 128 // GCOLS):
                    pe.wait_ge(gram_copied, SLOTS * CHUNKS * q - (1 if i == 0 else 0))
                high, low = table_parts(N_EXTRA - extra(q) + i)
                for r in range(OH_ROWS):
                    for part in (high, low):
                        last = nc.tensor.matmul(
                            onehot_rows(i, 1), part[:, r * DIM:(r + 1) * DIM],
                            onehot[0:OH_PARTS, i % ONEHOT_BUFS, r, :], start=(r == 0 and part is high),
                            stop=(r == OH_ROWS - 1 and part is low))
                last.then_inc(onehot_used, 1)
                if i + 3 < N_ONEHOT + extra(q):
                    pe.wait_ge(onehot_made, products_before(q) + i + 2)
                    spread_ids(q, i + 3)

            def transpose_batch(q, b, i):
                if i == 0:
                    pe.wait_ge(gathered[b], 16 * (N_GATHERED * (q + 1) - N_EXTRA))
                uses = (SLOTS * q + b) * BANK_BATCHES[i % 2] + i // 2
                if not (isinstance(q, int) and uses == 0):
                    pe.wait_ge(bank_copied[i % 2], uses)
                for k in range(min(PER_BANK, N_GATHERED - extra(q) - i * PER_BANK)):
                    last = nc.tensor.transpose(ps_t[i % 2][:, k * TILE:(k + 1) * TILE],
                                               emb[:, b, i * PER_BANK + k, :], ident[:, :])
                last.then_inc(transposed, 1)

            def products_and_transposes(q, first=False):
                for i in range(N_ONEHOT + extra(q)):
                    onehot_product(q, i, first)
                    for k in batches_after(q, i):
                        transpose_batch(q, 0, k)

            def features_ready(q, b):
                for bank in range(2):
                    pe.wait_ge(bank_copied[bank], (SLOTS * q + b + 1) * BANK_BATCHES[bank])
                if b == 0:
                    pe.wait_ge(dense_copied, q + 1)
                    pe.wait_ge(products_copied, product_banks_before(q) + product_banks(q))

            def gram_chunk(q, b, c, first=False, final=False):
                n = b * CHUNKS + c
                if not (first and n < 2):
                    pe.wait_ge(gram_copied, SLOTS * CHUNKS * q + n - 1)
                if final and n >= 2:
                    pe.wait_ge(blocks_copied, n - 1)
                for k in range(CHUNK):
                    s = (c * CHUNK + k) * PACK
                    last = nc.tensor.matmul(ps_g[n % 2][:, k, 0:PACK * PAIR_G], featT[:, b, s:s + PACK, :],
                                            featT[:, b, s:s + PACK, 1:FEATURES], start=True, stop=True)
                last.then_inc(gram_made, 1)

            def split_products(out, w_high, w_low, x_high, x_low, first, final):
                nc.tensor.matmul(out, w_high, x_high, start=first, stop=False)
                nc.tensor.matmul(out, w_high, x_low, start=False, stop=False)
                return nc.tensor.matmul(out, w_low, x_high, start=False, stop=final)

            def layer1(q, m):
                if m >= 2:
                    pe.wait_ge(h1_copied, M1 * q + m - 1)
                for kt in range(KT1):
                    n = PAIR_ROWS if kt < PAIR_KT else 128
                    cols = slice(m * 128, (m + 1) * 128)
                    last = split_products(ps_m[m % 2][:, 0:GCOLS], w1_high[0:n, kt, cols], w1_low[0:n, kt, cols],
                                          x1_high[0:n, kt, :], x1_low[0:n, kt, :], kt == 0, kt == KT1 - 1)
                last.then_inc(h1_made, 1)

            def layer1_blocks(m):
                if m >= 2:
                    pe.wait_ge(h1_copied, M1 * (GROUPS - 1) + m - 1)
                cols = slice(m * 128, (m + 1) * 128)
                out = ps_m[m % 2][:, 0:GCOLS]
                split_products(out, w1_high[:, PAIR_KT, cols], w1_low[:, PAIR_KT, cols],
                               x1_high[:, PAIR_KT, :], x1_low[:, PAIR_KT, :], True, False)
                for kt in range(BLOCK_KT):
                    n = min(PACK, PAIR_G - kt * PACK) * ROWS
                    last = nc.tensor.matmul(out, w1_quads[0:n, kt, cols], blocks[0:n, kt, :], start=False,
                                            stop=(kt == BLOCK_KT - 1))
                last.then_inc(h1_made, 1)

            def layer2(q):
                def products(m, kts):
                    for kt in kts:
                        cols = slice(m * 128, (m + 1) * 128)
                        last = split_products(ps_m[m][:, 0:GCOLS], w2_high[:, kt, cols], w2_low[:, kt, cols],
                                              h1_high[:, kt, :], h1_low[:, kt, :], kt == 0, kt == M1 - 1)
                    return last
                pe.wait_ge(h1_low_made, M1 * (q + 1) - 1)
                products(0, range(M1 - 1))
                pe.wait_ge(h1_copied, M1 * (q + 1))
                products(1, range(M1 - 1))
                pe.wait_ge(h1_low_made, M1 * (q + 1))
                for m in range(M2):
                    products(m, [M1 - 1]).then_inc(h2_made, 1)

            def layer3(q, tiles):
                pe.wait_ge(bank_copied[T_BATCHES % 2], tiles * BANK_BATCHES[T_BATCHES % 2])
                pe.wait_ge(h2_copied, M2 * (q + 1))
                for b in range(SLOTS):
                    for kt in range(M2):
                        last = nc.tensor.matmul(ps_y[:, b:b + 1], h2[:, kt, b * TILE:(b + 1) * TILE],
                                                w3_sb[:, kt:kt + 1], start=(kt == 0), stop=(kt == M2 - 1))
                last.then_inc(y_made, 1)

            def first_layer_and_transposes(q, scores=True):
                if scores:
                    pe.wait_ge(y_copied, q - 1)
                for i in range(2):
                    transpose_batch(q, 1, i)
                pe.wait_ge(x1_high_made, SLOTS * q)
                pe.wait_ge(x1_low_made, SLOTS * q)
                pe.wait_ge(dense_high, q)
                pe.wait_ge(dense_low, q)
                for m in range(M1):
                    layer1(q - 1, m)
                    if 2 + m < T_BATCHES:
                        transpose_batch(q, 1, 2 + m)

            def group(q, mlp=True, scores=True):
                first = isinstance(q, int) and q == 0
                products_and_transposes(q, first)
                if scores:
                    layer3(q - 2, SLOTS * q + 1)
                features_ready(q, 0)
                for c in range(CHUNKS):
                    gram_chunk(q, 0, c, first)
                if mlp:
                    first_layer_and_transposes(q, scores)
                    layer2(q - 1)
                else:
                    for i in range(T_BATCHES):
                        transpose_batch(q, 1, i)
                features_ready(q, 1)
                for c in range(CHUNKS):
                    gram_chunk(q, 1, c)
                    if c == 0:
                        if mlp:
                            pe.wait_ge(h2_copied, M2 * q)
                        pe.wait_ge(ids_casted, q + 2)
                        for i in range(2):
                            spread_ids(q + 1, i)
                    if c == 2:
                        spread_third_ids(q + 1)

            pe.wait_ge(ident_ready, 2)
            pe.wait_ge(setup_done, 3)
            pe.wait_ge(ids_casted, 1)
            for i in range(2):
                spread_ids(0, i)
            spread_third_ids(0)
            group(0, mlp=False, scores=False)
            pe.wait_ge(unit_high, UNITS)
            pe.wait_ge(unit_low, UNITS)
            group(1, scores=False)
            with pe.Fori(2, GROUPS - 1) as q:
                group(q)

            q = GROUPS - 1
            products_and_transposes(q)
            layer3(q - 2, SLOTS * q + 1)
            features_ready(q, 0)
            for c in range(CHUNKS):
                gram_chunk(q, 0, c, final=True)
            first_layer_and_transposes(q)
            features_ready(q, 1)
            for c in range(CHUNKS):
                gram_chunk(q, 1, c, final=True)
            layer2(q - 1)
            pe.wait_ge(dense_high, GROUPS)
            pe.wait_ge(dense_low, GROUPS)
            pe.wait_ge(blocks_weights_loaded, 16)
            pe.wait_ge(gram_copied, N_TILES * CHUNKS)
            pe.wait_ge(blocks_copied, SLOTS * CHUNKS)
            for m in range(M1):
                if m < M2:
                    pe.wait_ge(h2_copied, M2 * (q - 1) + m + 1)
                layer1_blocks(m)
                if m == 0:
                    layer3(q - 1, N_TILES)
            layer2(q)
            pe.wait_ge(y_copied, q)
            layer3(q, N_TILES)

        @block.vector
        def _(dve):
            def cast_ids(q):
                src = ids_all[:, bass.ds(q * SLOTS * N_TABLES, SLOTS * N_TABLES)].rearrange("p (b f) -> p b f", b=SLOTS)
                nc.vector.tensor_copy(ids_cast[:, :, :], src[:, :, N_GATHERED - N_EXTRA:N_TABLES])\
                    .then_inc(ids_casted, 1)

            def make_onehot(q, i):
                dve.wait_ge(ids_spread, products_before(q) + i + 1)
                if i >= ONEHOT_BUFS:
                    dve.wait_ge(onehot_used, products_before(q) + i - ONEHOT_BUFS + 1)
                elif not (isinstance(q, int) and q == 0):
                    n = N_ONEHOT + (extra(q - 1) if isinstance(q, int) else 0)
                    last = (n - 1 - i) // ONEHOT_BUFS * ONEHOT_BUFS + i
                    dve.wait_ge(onehot_used, products_before(q - 1) + last + 1)
                nc.vector.tensor_tensor(
                    onehot[:, i % ONEHOT_BUFS, :, :],
                    ps_m[i % 2][:, 0:GCOLS].unsqueeze(1).to_broadcast([128, OH_ROWS, GCOLS]),
                    row_id[:, :].unsqueeze(2).to_broadcast([128, OH_ROWS, GCOLS]), ALU.is_equal)\
                    .then_inc(onehot_made, 1)

            def copy_transposes(q, i):
                bank, src, dst = transposed_batch(q, 1, i)
                dve.wait_ge(transposed, T_BATCHES * (SLOTS * q + 1) + i + 1)
                nc.vector.tensor_copy(dst, src).then_inc(bank_copied[bank], 1)

            def copy_blocks(n):
                dve.wait_ge(gram_made, SLOTS * CHUNKS * (GROUPS - 1) + n + 1)
                for s in range(PACK // 2, PACK):
                    for j in range(PACK):
                        dst, src = block_move(n, s, j)
                        last = nc.vector.tensor_copy(dst, src)
                last.then_inc(blocks_copied, 1)

            def split_x1(q, b):
                dve.wait_ge(x1_high_made, SLOTS * q + b + 1)
                at = pairs_of(b)
                nc.vector.tensor_sub(x1_low[at], x1[at], x1_high[at].bitcast(fp32)).then_inc(x1_low_made, 1)

            def split_dense(q):
                dve.wait_ge(dense_high, q + 1)
                nc.vector.tensor_sub(x1_low[:, PAIR_KT, :], x1[:, PAIR_KT, :],
                                     x1_high[:, PAIR_KT, :].bitcast(fp32)).then_inc(dense_low, 1)

            def split_h1(q, m):
                dve.wait_ge(h1_copied, M1 * q + m + 1)
                nc.vector.tensor_sub(h1_low[:, m, :], h1[:, m % 2, :],
                                     h1_high[:, m, :].bitcast(fp32)).then_inc(h1_low_made, 1)

            def first_layer_and_transposes(q, mlp=True):
                for i in range(2):
                    copy_transposes(q, i)
                for m in range(M1):
                    if mlp:
                        split_h1(q - 1, m)
                    if 2 + m < T_BATCHES:
                        copy_transposes(q, 2 + m)
                split_dense(q)

            def group(q, mlp=True):
                if mlp:
                    for i in range(ONEHOT_BUFS, N_ONEHOT):
                        make_onehot(q, i)
                cast_ids(q + 1)
                if mlp:
                    for b in range(SLOTS):
                        split_x1(q - 1, b)
                first_layer_and_transposes(q, mlp)
                for i in range(ONEHOT_BUFS):
                    make_onehot(q + 1, i)

            nc.vector.memset(featT[:, :, :, FEATURES:ROWS], 0.0).then_inc(setup_done, 1)
            dve.wait_ge(row_ids_made, 1)
            nc.vector.tensor_copy(row_id[:, :], row_id_int[:, :]).then_inc(setup_done, 1)
            dve.wait_ge(ident_ready, 2)
            nc.vector.tensor_copy(ident_r[:, :], ident[:, :]).then_inc(setup_done, 1)
            dve.wait_ge(ids_loaded, 16)
            dve.wait_ge(setup_done, 3)
            cast_ids(0)
            make_onehot(0, 0)
            for u in range(UNITS):
                if u + 1 < N_EXTRA + N_ONEHOT:
                    make_onehot(0, u + 1)
                dve.wait_ge(unit_high, u + 1)
                _, high, low = unit(u)
                nc.vector.tensor_sub(low, staged(u, low), high.bitcast(fp32)).then_inc(unit_low, 1)
            group(0, mlp=False)
            with dve.Fori(1, GROUPS - 1) as q:
                group(q)

            q = GROUPS - 1
            for i in range(ONEHOT_BUFS, N_ONEHOT):
                make_onehot(q, i)
            split_x1(q - 1, 0)
            for c in range(CHUNKS):
                if c == CHUNKS - 2:
                    split_x1(q - 1, 1)
                copy_blocks(c)
            first_layer_and_transposes(q)
            for c in range(CHUNKS):
                copy_blocks(CHUNKS + c)
            for m in range(M1):
                split_h1(q, m)

        @block.scalar
        def _(act):
            with nc.allow_non_contiguous_dma(reason="768 bias values, once"):
                act.dma_start(b1_sb[:, :], b1.rearrange("(m p) -> p m", p=128)).then_inc(biases_loaded, 16)
                act.dma_start(b2_sb[:, :], b2.rearrange("(m p) -> p m", p=128)).then_inc(biases_loaded, 16)
                act.dma_start(w3_sb[:, :], w3.rearrange("(m p) o -> p (m o)", p=128)).then_inc(biases_loaded, 16)

            def split_unit(u):
                act.wait_ge(unit_loaded[u], 16)
                _, high, _ = unit(u)
                nc.scalar.activation(high, staged(u, high), ACT.Copy).then_inc(unit_high, 1)

            for u in range(N_EXTRA + N_ONEHOT):
                split_unit(u)

            def copy_product(q, j):
                k = min(OH_PER_BANK, N_ONEHOT + extra(q) - OH_PER_BANK * j)
                act.wait_ge(onehot_used, products_before(q) + OH_PER_BANK * j + k)
                nc.scalar.activation(
                    features(SPLIT - extra(q) + OH_PER_BANK * j, k),
                    onehot_rows(OH_PER_BANK * j, k).rearrange("d (f b s) -> d f b s", f=k, b=SLOTS),
                    ACT.Copy).then_inc(products_copied, 1)

            def copy_transposes(q, i):
                bank, src, dst = transposed_batch(q, 0, i)
                act.wait_ge(transposed, T_BATCHES * SLOTS * q + i + 1)
                nc.scalar.activation(dst, src, ACT.Copy).then_inc(bank_copied[bank], 1)

            def copy_first_half(q):
                act.wait_ge(dense_loaded, 16 * (q + 1))
                nc.scalar.activation(featT[:, :, :, 0], x1[:, PAIR_KT, :].rearrange("d (b s) -> d b s", b=SLOTS),
                                     ACT.Copy).then_inc(dense_copied, 1)
                for i in range(N_ONEHOT + extra(q)):
                    if isinstance(q, int) and q == 0 and i % 2 == 0 and i // 2 < UNITS - N_EXTRA - N_ONEHOT:
                        split_unit(N_EXTRA + N_ONEHOT + i // 2)
                    if i % OH_PER_BANK == OH_PER_BANK - 1 or i == N_ONEHOT + extra(q) - 1:
                        copy_product(q, i // OH_PER_BANK)
                    for k in batches_after(q, i):
                        copy_transposes(q, k)

            def copy_gram(q, b, c):
                n = b * CHUNKS + c
                act.wait_ge(gram_made, SLOTS * CHUNKS * q + n + 1)
                cols = gram[:, :, b * TILE + c * CHUNK * PACK:b * TILE + (c + 1) * CHUNK * PACK]
                cols = cols.rearrange("f g (k s) -> f s k g", s=PACK)
                for s in range(PACK):
                    last = nc.scalar.activation(
                        cols[:, s, :, :], ps_g[n % 2][s * ROWS:s * ROWS + PAIR_G, :, s * PAIR_G:(s + 1) * PAIR_G],
                        ACT.Copy)
                last.then_inc(gram_copied, 1)

            def copy_blocks(n):
                act.wait_ge(gram_made, SLOTS * CHUNKS * (GROUPS - 1) + n + 1)
                for s in range(PACK // 2):
                    for j in range(PACK):
                        dst, src = block_move(n, s, j)
                        last = nc.scalar.activation(dst, src, ACT.Copy)
                last.then_inc(gram_copied, 1)

            def split_x1(q, b):
                if isinstance(q, int) and q == 0 and b == 0:
                    act.wait_ge(both_packed, 16 * (len(MOVES) - EARLY_MOVES))
                act.wait_ge(x1_packed[b], 16 * (len(MOVES) * q + EARLY_MOVES))
                at = pairs_of(b)
                nc.scalar.activation(x1_high[at], x1[at], ACT.Copy).then_inc(x1_high_made, 1)

            def split_dense():
                nc.scalar.activation(x1_high[:, PAIR_KT, :], x1[:, PAIR_KT, :], ACT.Copy).then_inc(dense_high, 1)

            def relu1(q, first=False):
                for m in range(M1):
                    act.wait_ge(h1_made, M1 * q + m + 1)
                    if not (first and m < 2):
                        act.wait_ge(h1_low_made, M1 * q + m - 1)
                    nc.scalar.activation(h1[:, m % 2, :], ps_m[m % 2][:, 0:GCOLS], ACT.Relu, bias=b1_sb[:, m:m + 1])
                    nc.scalar.activation(h1_high[:, m, :], ps_m[m % 2][:, 0:GCOLS], ACT.Relu,
                                         bias=b1_sb[:, m:m + 1]).then_inc(h1_copied, 1)

            def relu2(q):
                for m in range(M2):
                    act.wait_ge(h2_made, M2 * q + m + 1)
                    nc.scalar.activation(h2[:, m, :], ps_m[m % 2][:, 0:GCOLS], ACT.Relu,
                                         bias=b2_sb[:, m:m + 1]).then_inc(h2_copied, 1)

            def copy_scores(q):
                act.wait_ge(y_made, q + 1)
                nc.scalar.activation(y[:, bass.ds(q * SLOTS, SLOTS)], ps_y[:, 0:SLOTS], ACT.Copy)\
                    .then_inc(y_copied, 1)

            def group(q, mlp=True, scores=True):
                copy_first_half(q)
                if mlp:
                    split_x1(q - 1, 0)
                if scores:
                    copy_scores(q - 2)
                if not mlp:
                    act.wait_ge(unit_low, UNITS)
                for c in range(CHUNKS):
                    if c == CHUNKS - 2 and mlp:
                        split_x1(q - 1, 1)
                    copy_gram(q, 0, c)
                if mlp:
                    relu1(q - 1, first=not scores)
                split_dense()
                if mlp:
                    relu2(q - 1)
                for c in range(CHUNKS):
                    copy_gram(q, 1, c)

            group(0, mlp=False, scores=False)
            act.wait_ge(biases_loaded, 48)
            group(1, scores=False)
            with act.Fori(2, GROUPS - 1) as q:
                group(q)

            q = GROUPS - 1
            copy_first_half(q)
            split_x1(q - 1, 0)
            copy_scores(q - 2)
            for c in range(CHUNKS):
                if c == CHUNKS - 2:
                    split_x1(q - 1, 1)
                copy_blocks(c)
            act.dma_start(w1_quads[:, :, :], w1_blocks.rearrange("(k p) n -> p k n", p=128))\
                .then_inc(blocks_weights_loaded, 16)
            relu1(q - 1)
            split_dense()
            for c in range(CHUNKS):
                copy_blocks(CHUNKS + c)
            relu2(q - 1)
            copy_scores(q - 1)
            relu1(q)
            relu2(q)
            copy_scores(q)


def kernel(**inputs):
    import numpy as _np
    import concourse.bacc as _bacc
    from concourse import mybir as _mybir
    from concourse.bass_utils import run_bass_kernel_spmd as _run

    nc = _bacc.Bacc("TRN2", target_bir_lowering=False, num_devices=1)
    by_tile = _np.asarray(inputs["r_dense_features"]).reshape(TILE, N_TILES, DIM).transpose(2, 1, 0)
    inputs["dense_t"] = by_tile.reshape(DIM, BATCH)
    names = ["dense_t", "ids"] + [f"tbl_{f}" for f in range(N_TABLES)]
    names += ["W_top1", "b_top1", "W_top2", "b_top2", "W_top3"]
    arrays, args = {}, {}
    for name in names:
        a = inputs[name]
        if name == "ids":
            a = a[:, TABLE_ORDER]
        if name == "W_top1":
            rows = _np.zeros((BLOCK_KT * PACK, ROWS, HIDDEN1), a.dtype)
            for g in range(PAIR_G):
                rows[g, 0:g + 1] = a[[pair_row(f, g) for f in range(g + 1)]]
            blocks = rows.reshape(BLOCK_KT * 128, HIDDEN1)
            arrays["in_w1_blocks_dram"] = blocks
            args["w1_blocks"] = nc.dram_tensor("in_w1_blocks_dram", blocks.shape, _mybir.dt.from_np(blocks.dtype),
                                               kind="ExternalInput").ap()
            a = a[w1_rows()]
        a = _np.ascontiguousarray(a)
        arrays[f"in_{name}_dram"] = a
        args[name] = nc.dram_tensor(f"in_{name}_dram", a.shape, _mybir.dt.from_np(a.dtype), kind="ExternalInput").ap()
    out = nc.dram_tensor("out_0_dram", (BATCH, 1), _mybir.dt.float32, kind="ExternalOutput").ap()
    build(nc, args["dense_t"], args["ids"], [args[f"tbl_{f}"] for f in range(N_TABLES)],
          args["W_top1"], args["w1_blocks"], args["b_top1"], args["W_top2"], args["b_top2"], args["W_top3"], out)
    r = _run(nc, [arrays], core_ids=[0])
    return r.results[0]["out_0_dram"]
```
